# Optimizing a Trainium2 kernel written in Bass

```python
import numpy as np
import jax
import jax.numpy as jnp

def _softmax(x, axis=-1):
    return jax.nn.softmax(x, axis=axis)

def _gelu(x):
    return jax.nn.gelu(x, approximate=True)

def _silu(x):
    return jax.nn.silu(x)

def _sigmoid(x):
    return jax.nn.sigmoid(x)

def _layernorm(x, axis=-1, eps=1e-05):
    m = jnp.mean(x, axis=axis, keepdims=True)
    v = jnp.var(x, axis=axis, keepdims=True)
    return (x - m) / jnp.sqrt(v + eps)

def _scatter_add(tgt, idx, src, axis=0):
    return tgt.at[idx].add(src)

def _segment_sum(src, seg, n):
    return jax.ops.segment_sum(src, seg, n)
kernel_name = 'mk_adj_preln_d1_adj_r2_75d04e'

def setup_inputs(seed: int=0):
    np.random.seed(seed)
    _w = jnp.asarray

    def _rec_inputs():
        import jax
        import jax.numpy as jnp
        _gk = jax.random.key(seed)
        x = -0.0005207 + 1.001 * jax.random.normal(jax.random.fold_in(_gk, 1), (8192, 128), jnp.float32)
        _a = jax.random.bernoulli(jax.random.fold_in(_gk, 2), 0.000488281, (8192, 8192))
        _a = jnp.logical_or(_a, jnp.eye(8192, dtype=bool))
        _af = _a.astype(jnp.float32)
        _af = _af * jax.random.uniform(jax.random.fold_in(_gk, 3), (8192, 8192), jnp.float32, 0.05, 1)
        adj = _af
        return (x, adj)
    x, adj = _rec_inputs()

    def _L0_gnn_setup():
        import jax, jax.numpy as jnp
        import numpy as np
        N = 8192
        F_IN = 128
        F_OUT = 128
        key = jax.random.key(seed)
        k1, k2, k3, k4 = jax.random.split(key, 4)
        x = jax.random.normal(k1, (N, F_IN), dtype=jnp.float32)
        adj = jax.random.uniform(k2, (N, N), dtype=jnp.float32)
        bound = 1.0 / np.sqrt(2 * F_IN)
        W = jax.random.uniform(k3, (F_OUT, 2 * F_IN), minval=-bound, maxval=bound, dtype=jnp.float32)
        b = jax.random.uniform(k4, (F_OUT,), minval=-bound, maxval=bound, dtype=jnp.float32)
        return {'x': x, 'adj': adj, 'W': W, 'b': b}
    _L0_gnn_all = _L0_gnn_setup()
    _L0_gnn_in = {k: v for k, v in _L0_gnn_all.items() if k in ('W', 'b')}
    del _L0_gnn_all
    return {'x': x, 'adj': adj, 'L0_gnn_W': _L0_gnn_in['W'], 'L0_gnn_b': _L0_gnn_in['b']}

def reference(x, adj, L0_gnn_W, L0_gnn_b):
    import jax
    import jax.numpy as jnp

    def _L0_gnn_ref(x, adj, W, b):
        import jax, jax.numpy as jnp
        import numpy as np
        N = 8192
        F_IN = 128
        F_OUT = 128
        neigh = adj @ x
        W_self = W[:, :F_IN]
        W_neigh = W[:, F_IN:]
        return x @ W_self.T + neigh @ W_neigh.T + b
    h = jnp.maximum(_layernorm(x, axis=-1), 0.0)
    x = x + _L0_gnn_ref(h, adj, L0_gnn_W, L0_gnn_b)
    return x

_drawn_inputs = setup_inputs


def setup_inputs(seed=0):
    import zlib

    import numpy as np

    out = dict(_drawn_inputs(seed))
    spreads = {}
    factors = {}
    for name, (base, spread) in spreads.items():
        noise = np.random.default_rng([zlib.crc32(name.encode()), seed]).standard_normal(out[name].shape)
        drawn = base * np.exp(spread * noise) if base else spread * noise
        out[name] = jnp.asarray(drawn.astype(out[name].dtype))
    for name, factor in factors.items():
        out[name] = (out[name] * factor).astype(out[name].dtype)
    return out
```

```python
from contextlib import ExitStack

import concourse.bass as bass
from concourse import mybir

F32 = mybir.dt.float32
F32R = mybir.dt.float32r
ALU = mybir.AluOpType
ACT = mybir.ActivationFunctionType

P = 128
N = 8192
D = 128
EPS = 1e-5
BANK = 512
TILES = N // P
CHUNK = 2048
PER = CHUNK // BANK
GROUPS = TILES // PER
WIDE = CHUNK // BANK
NARROW = GROUPS - WIDE
STRIP_CHUNKS = TILES // PER
UNROLL = 3
BODY = UNROLL * STRIP_CHUNKS
ROUNDS = NARROW // UNROLL
RAW = 6
HI = 3
LO = 2
STAGES = 2
SLOTS = 3
assert BODY % RAW == BODY % HI == BODY % LO == 0 and ROUNDS * UNROLL == NARROW

STATS = [(0, 4, None, 4), (4, 16, 0, 12), (16, 32, 2, 2), (32, 48, 10, 1), (48, 64, 26, 1)]


def gathered(i):
    a, b, first, rate = STATS[i]
    return first + (b - a) // rate - 1


def slot_of(strip):
    return (strip - WIDE) % SLOTS


def graph_layer(nc, x, adj, w_t, bias, out):
    with ExitStack() as ctx:
        def sb(name, shape, dt=F32):
            return ctx.enter_context(nc.sbuf_tensor(name, shape, dt))

        def sem(name):
            return ctx.enter_context(nc.semaphore(name))

        base = sb("base", [P, TILES, D])
        h_hi = sb("h_hi", [P, TILES, D], F32R)
        h_lo = sb("h_lo", [P, TILES, D], F32R)
        raw = sb("raw", [P, RAW, CHUNK])
        a_hi = sb("a_hi", [P, HI, CHUNK], F32R)
        a_lo = sb("a_lo", [P, LO, CHUNK], F32R)
        h = sb("h", [P, STAGES, PER, D])
        h_t = sb("h_t", [P, PER * P])
        self_sb = sb("self_sb", [P, PER, D])
        strip_sb = sb("strip_sb", [P, SLOTS, BANK])
        w_self = sb("w_self", [P, D])
        w_neigh = sb("w_neigh", [P, D])
        bias_rows = sb("bias_rows", [P, D])
        identity = sb("identity", [P, P])
        moments = sb("moments", [P, TILES, 6])
        mean_var = sb("mean_var", [P, TILES, 2])
        var_eps = sb("var_eps", [P, TILES])
        std = sb("std", [P, TILES])
        guess = sb("guess", [P, TILES])
        scratch = sb("scratch", [P, TILES])
        rstd = sb("rstd", [P, TILES])
        shift = sb("shift", [P, TILES])

        psum = [ctx.enter_context(nc.psum_tensor(f"bank{i}", [P, BANK], F32)) for i in range(8)]
        acc = [psum[slot_of(strip)] if strip else psum[SLOTS] for strip in range(WIDE + UNROLL)]
        project_ps = psum[4:4 + SLOTS]
        turned_ps = psum[6]
        self_ps = psum[7]

        x_loaded = [sem(f"x_loaded{i}") for i in range(len(STATS))]
        consts_loaded = sem("consts_loaded")
        raw_loaded = [sem(f"raw_loaded{i}") for i in range(RAW)]
        out_stored = [sem(f"out_stored{i}") for i in range(SLOTS)]
        identity_zero = sem("identity_zero")
        identity_ready = sem("identity_ready")
        moments_ready = sem("moments_ready")
        mean_var_ready = sem("mean_var_ready")
        var_ready = sem("var_ready")
        std_ready = sem("std_ready")
        newton_step = sem("newton_step")
        norm_ready = sem("norm_ready")
        h_ready = sem("h_ready")
        h_hi_ready = sem("h_hi_ready")
        h_lo_ready = sem("h_lo_ready")
        turned = sem("turned")
        h_t_ready = sem("h_t_ready")
        self_done = sem("self_done")
        self_out = sem("self_out")
        base_step = sem("base_step")
        base_ready = sem("base_ready")
        hi_ready = sem("hi_ready")
        lo_ready = sem("lo_ready")
        chunk_used = sem("chunk_used")
        neigh_ready = sem("neigh_ready")
        projected = sem("projected")
        out_ready = sem("out_ready")

        block = ctx.enter_context(nc.Block())

        @block.sync
        def _(sp):
            def load_x(i):
                a, b, _, _ = STATS[i]
                sp.dma_start(base[:, a:b, :], x[:, a:b, :]).then_inc(x_loaded[i], 16)

            def load_chunk(c, slot, wait):
                if wait:
                    sp.wait_ge(lo_ready, c - RAW + 1)
                sp.dma_start(raw[:, slot, :], adj[c, :, :]).then_inc(raw_loaded[slot], 16)

            def store(strip, slot):
                sp.wait_ge(out_ready, strip + 1)
                sp.dma_start(out[strip, :, :], strip_sb[:, slot, :]).then_inc(out_stored[slot], 16)

            load_x(0)
            for c in range(TILES):
                load_chunk(c, c % RAW, c >= RAW)
                if c < 2 * len(STATS) - 2 and c % 2 == 0:
                    load_x(c // 2 + 1)
            for strip in range(WIDE - 1):
                store(strip, slot_of(strip))
            with sp.Fori(0, ROUNDS) as r:
                for u in range(UNROLL):
                    for k in range(STRIP_CHUNKS):
                        n = TILES + u * STRIP_CHUNKS + k
                        load_chunk(r * BODY + n, n % RAW, True)
                        if k == STRIP_CHUNKS - 4:
                            store(r * UNROLL + (WIDE + u - 1), slot_of(WIDE + u - 1))
            store(GROUPS - 1, slot_of(GROUPS - 1))
            for slot in range(SLOTS):
                sp.wait_ge(out_stored[slot], 16 * len([s for s in range(GROUPS) if slot_of(s) == slot]))

        @block.gpsimd
        def _(pool):
            nc.gpsimd.memset(identity[:], 0.0).then_inc(identity_zero, 1)
            pool.wait_ge(identity_zero, 1)
            nc.gpsimd.affine_select(out=identity[:], in_=identity[:], compare_op=ALU.not_equal, fill=1.0,
                                    base=0, pattern=[[-1, P]], channel_multiplier=1).then_inc(identity_ready, 1)
            pool.wait_ge(consts_loaded, 16 * 3)
            for g in range(GROUPS):
                rows = base[:, g * PER:(g + 1) * PER, :]
                pool.wait_ge(self_out, g + 1)
                nc.gpsimd.tensor_tensor(rows, rows, self_sb[:], ALU.add).then_inc(base_step, 1)
                pool.wait_ge(base_step, g + 1)
                for t in range(PER):
                    row = base[:, g * PER + t, :]
                    last = nc.gpsimd.tensor_tensor(row, row, bias_rows[:], ALU.add)
                last.then_inc(base_ready, 1)

        @block.scalar
        def _(act):
            act.dma_start(w_self[:], w_t[0:D, :]).then_inc(consts_loaded, 16)
            act.dma_start(w_neigh[:], w_t[D:2 * D, :]).then_inc(consts_loaded, 16)
            act.dma_start(bias_rows[:], bias.to_broadcast([P, D])).then_inc(consts_loaded, 16)

            def split_hi(c, raw_slot, loads, hi_slot, wait):
                act.wait_ge(raw_loaded[raw_slot], loads)
                if wait:
                    act.wait_ge(chunk_used, c - HI + 1)
                nc.scalar.copy(a_hi[:, hi_slot, :], raw[:, raw_slot, :]).then_inc(hi_ready, 1)

            def root(i):
                a, b, _, _ = STATS[i]
                act.wait_ge(var_ready, i + 1)
                nc.scalar.activation(std[:, a:b], var_eps[:, a:b], ACT.Sqrt).then_inc(std_ready, 1)

            def normalise(g):
                i = [n for n, (a, b, _, _) in enumerate(STATS) if a <= g * PER < b][0]
                act.wait_ge(norm_ready, i + 1)
                if g >= STAGES:
                    act.wait_ge(turned, g - STAGES + 1)
                    act.wait_ge(h_lo_ready, g - STAGES + 1)
                for n in range(PER):
                    t = g * PER + n
                    last = nc.scalar.activation(h[:, g % STAGES, n, :], base[:, t, :], ACT.Relu,
                                                bias=shift[:, t:t + 1], scale=rstd[:, t:t + 1])
                last.then_inc(h_ready, 1)
                act.wait_ge(h_ready, g + 1)
                nc.scalar.copy(h_hi[:, g * PER:(g + 1) * PER, :], h[:, g % STAGES, :, :]).then_inc(h_hi_ready, 1)

            def bring_self(g):
                act.wait_ge(self_done, g + 1)
                if g:
                    act.wait_ge(base_step, g)
                nc.scalar.copy(self_sb[:], self_ps[:].rearrange("p (t d) -> p t d", t=PER)).then_inc(self_out, 1)

            def bring_h_t(g):
                act.wait_ge(turned, g + 1)
                if g:
                    act.wait_ge(self_done, g)
                nc.scalar.copy(h_t[:], turned_ps[:]).then_inc(h_t_ready, 1)

            def bring_neigh(slot, bank, chunks, stores):
                act.wait_ge(chunk_used, chunks)
                if stores is not None:
                    act.wait_ge(out_stored[slot], stores)
                nc.scalar.copy(strip_sb[:, slot, :], bank[:]).then_inc(neigh_ready, 1)

            root(0)
            normalise(0)
            for c in range(TILES):
                split_hi(c, c % RAW, 16 * (c // RAW + 1), c % HI, c >= HI)
                g, step = divmod(c, PER)
                for i in range(1, len(STATS)):
                    if c == gathered(i) + (0 if i == 1 else 2):
                        root(i)
                if step == 2 and g + 1 < GROUPS:
                    normalise(g + 1)
                if step == 3:
                    if g:
                        bring_self(g - 1)
                    bring_h_t(g)
            bring_self(GROUPS - 1)
            for strip in range(WIDE - 1):
                bring_neigh(slot_of(strip), acc[strip], TILES, None)
            with act.Fori(0, ROUNDS) as r:
                for u in range(UNROLL):
                    for k in range(STRIP_CHUNKS):
                        n = TILES + u * STRIP_CHUNKS + k
                        split_hi(r * BODY + n, n % RAW, r * (16 * BODY // RAW) + 16 * (n // RAW + 1), n % HI, True)
                        if k == 1:
                            before = WIDE + u - 1
                            bring_neigh(slot_of(before), acc[before], r * BODY + (TILES + u * STRIP_CHUNKS),
                                        r * 16 + 16 * (before // SLOTS))
            bring_neigh(slot_of(GROUPS - 1), acc[WIDE + UNROLL - 1], TILES + ROUNDS * BODY,
                        16 * ((GROUPS - 1) // SLOTS))


        @block.vector
        def _(dve):
            def split_lo(c, raw_slot, hi_slot, lo_slot, wait):
                dve.wait_ge(hi_ready, c + 1)
                if wait:
                    dve.wait_ge(chunk_used, c - LO + 1)
                nc.vector.tensor_tensor(a_lo[:, lo_slot, :], raw[:, raw_slot, :],
                                        a_hi[:, hi_slot, :].bitcast(F32), ALU.subtract).then_inc(lo_ready, 1)

            def gather(a, b):
                for t in range(a, b):
                    last = nc.vector.bn_stats(moments[:, t, :], base[:, t, :])
                last.then_inc(moments_ready, b - a)
                dve.wait_ge(moments_ready, b)
                for t in range(a, b):
                    last = nc.vector.bn_aggr(mean_var[:, t, :], moments[:, t, :])
                last.then_inc(mean_var_ready, b - a)

            def add_eps(i):
                a, b, _, _ = STATS[i]
                dve.wait_ge(mean_var_ready, b)
                nc.vector.tensor_scalar(var_eps[:, a:b], mean_var[:, a:b, 1], EPS, None, ALU.add).then_inc(var_ready, 1)

            def invert(i):
                a, b, _, _ = STATS[i]
                v, y, s = var_eps[:, a:b], guess[:, a:b], scratch[:, a:b]
                dve.wait_ge(std_ready, i + 1)
                nc.vector.reciprocal(y, std[:, a:b]).then_inc(newton_step, 1)
                dve.wait_ge(newton_step, 5 * i + 1)
                nc.vector.tensor_tensor(s, v, y, ALU.mult).then_inc(newton_step, 1)
                dve.wait_ge(newton_step, 5 * i + 2)
                nc.vector.tensor_tensor(s, s, y, ALU.mult).then_inc(newton_step, 1)
                dve.wait_ge(newton_step, 5 * i + 3)
                nc.vector.tensor_scalar(s, s, -0.5, 1.5, ALU.mult, ALU.add).then_inc(newton_step, 1)
                dve.wait_ge(newton_step, 5 * i + 4)
                nc.vector.tensor_tensor(rstd[:, a:b], y, s, ALU.mult).then_inc(newton_step, 1)
                dve.wait_ge(newton_step, 5 * i + 5)
                nc.vector.scalar_tensor_tensor(out=shift[:, a:b], in0=mean_var[:, a:b, 0], scalar=-1.0,
                                               in1=rstd[:, a:b], op0=ALU.mult, op1=ALU.mult).then_inc(norm_ready, 1)

            def normalised_lo(g):
                dve.wait_ge(h_hi_ready, g + 1)
                tiles = slice(g * PER, (g + 1) * PER)
                nc.vector.tensor_tensor(h_lo[:, tiles, :], h[:, g % STAGES, :, :], h_hi[:, tiles, :].bitcast(F32),
                                        ALU.subtract).then_inc(h_lo_ready, 1)

            def add_up(strip, slot):
                dve.wait_ge(projected, strip + 1)
                tiles = base[:, bass.ds(strip * PER, PER), :]
                nc.vector.tensor_tensor(strip_sb[:, slot, :].rearrange("p (t d) -> p t d", t=PER),
                                        project_ps[slot][:].rearrange("p (t d) -> p t d", t=PER),
                                        tiles, ALU.add).then_inc(out_ready, 1)

            dve.wait_ge(x_loaded[0], 16)
            gather(*STATS[0][:2])
            add_eps(0)
            invert(0)
            normalised_lo(0)
            for c in range(TILES):
                split_lo(c, c % RAW, c % HI, c % LO, c >= LO)
                g, step = divmod(c, PER)
                for i in range(1, len(STATS)):
                    a, b, first, rate = STATS[i]
                    if first <= c <= gathered(i):
                        if c == first:
                            dve.wait_ge(x_loaded[i], 16)
                        gather(a + (c - first) * rate, a + (c - first + 1) * rate)
                    if c == gathered(i):
                        add_eps(i)
                    if c == gathered(i) + (0 if i == 1 else 3):
                        invert(i)
                if step == 2 and g + 1 < GROUPS:
                    normalised_lo(g + 1)
            dve.wait_ge(base_ready, GROUPS)
            for strip in range(WIDE - 1):
                add_up(strip, slot_of(strip))
            with dve.Fori(0, ROUNDS) as r:
                for u in range(UNROLL):
                    for k in range(STRIP_CHUNKS):
                        n = TILES + u * STRIP_CHUNKS + k
                        split_lo(r * BODY + n, n % RAW, n % HI, n % LO, True)
                        if k == 5:
                            before = WIDE + u - 1
                            add_up(r * UNROLL + before, slot_of(before))
            add_up(GROUPS - 1, slot_of(GROUPS - 1))

        @block.tensor
        def _(pe):
            def products(c, hi_slot, lo_slot, terms):
                pe.wait_ge(hi_ready, c + 1)
                for n, (tile, bank, first, _) in enumerate(terms):
                    nc.tensor.matmul(bank[:], h_hi[:, tile, :], a_hi[:, hi_slot, n * BANK:(n + 1) * BANK],
                                     start=first, stop=False)
                for n, (tile, bank, _, _) in enumerate(terms):
                    nc.tensor.matmul(bank[:], h_lo[:, tile, :], a_hi[:, hi_slot, n * BANK:(n + 1) * BANK],
                                     start=False, stop=False)
                pe.wait_ge(lo_ready, c + 1)
                for n, (tile, bank, _, last) in enumerate(terms):
                    mm = nc.tensor.matmul(bank[:], h_hi[:, tile, :], a_lo[:, lo_slot, n * BANK:(n + 1) * BANK],
                                          start=False, stop=last)
                mm.then_inc(chunk_used, 1)

            def turn(g):
                pe.wait_ge(h_ready, g + 1)
                if g:
                    pe.wait_ge(h_t_ready, g)
                for t in range(PER):
                    last = nc.tensor.transpose(turned_ps[:, t * P:(t + 1) * P], h[:, g % STAGES, t, :], identity[:])
                last.then_inc(turned, 1)

            def self_term(g):
                pe.wait_ge(h_t_ready, g + 1)
                if g:
                    pe.wait_ge(self_out, g)
                for t in range(PER):
                    last = nc.tensor.matmul(self_ps[:, t * D:(t + 1) * D], h_t[:, t * P:(t + 1) * P], w_self[:],
                                            start=True, stop=True)
                last.then_inc(self_done, 1)

            def project(strip, slot, wait):
                pe.wait_ge(neigh_ready, strip + 1)
                if wait:
                    pe.wait_ge(out_ready, strip - SLOTS + 1)
                for t in range(PER):
                    last = nc.tensor.matmul(project_ps[slot][:, t * D:(t + 1) * D],
                                            strip_sb[:, slot, t * P:(t + 1) * P], w_neigh[:], start=True, stop=True)
                last.then_inc(projected, 1)

            pe.wait_ge(identity_ready, 1)
            turn(0)
            pe.wait_ge(consts_loaded, 16 * 3)
            pe.wait_ge(h_hi_ready, 1)
            pe.wait_ge(h_lo_ready, 1)
            for c in range(TILES):
                g, step = divmod(c, PER)
                if step == 0:
                    pe.wait_ge(h_hi_ready, g + 1)
                    pe.wait_ge(h_lo_ready, g + 1)
                products(c, c % HI, c % LO, [(c, acc[s], c == 0, c == TILES - 1) for s in range(WIDE)])
                if step == 3:
                    self_term(g)
                    if g + 1 < GROUPS:
                        turn(g + 1)
            for strip in range(WIDE - 1):
                project(strip, slot_of(strip), False)
            with pe.Fori(0, ROUNDS) as r:
                for u in range(UNROLL):
                    pe.wait_ge(neigh_ready, r * UNROLL + (u + WIDE - SLOTS + 1))
                    for k in range(STRIP_CHUNKS):
                        n = TILES + u * STRIP_CHUNKS + k
                        products(r * BODY + n, n % HI, n % LO,
                                 [(t, acc[WIDE + u], t == 0, t == TILES - 1) for t in range(k * PER, (k + 1) * PER)])
                        if k == 1:
                            before = WIDE + u - 1
                            project(r * UNROLL + before, slot_of(before), True)
            project(GROUPS - 1, slot_of(GROUPS - 1), True)


def kernel(x, adj, L0_gnn_W, L0_gnn_b):
    import numpy as np
    import concourse.bacc as bacc
    from concourse.bass_utils import run_bass_kernel_spmd

    x, adj, w, b = np.asarray(x), np.asarray(adj), np.asarray(L0_gnn_W), np.asarray(L0_gnn_b)
    wide = N // GROUPS * WIDE
    arrays = {
        "x": np.ascontiguousarray(x.reshape(TILES, P, D).transpose(1, 0, 2)),
        "adj": np.concatenate([
            adj[:wide].T.reshape(TILES, P, CHUNK),
            adj[wide:].reshape(NARROW, BANK, STRIP_CHUNKS, PER, P).transpose(0, 2, 4, 3, 1)
            .reshape(NARROW * STRIP_CHUNKS, P, CHUNK),
        ]),
        "w_t": np.ascontiguousarray(w.T),
        "bias": b.reshape(1, D),
    }
    nc = bacc.Bacc("TRN2", target_bir_lowering=False, num_devices=1)
    aps = {name: nc.dram_tensor(name + "_in", a.shape, F32, kind="ExternalInput").ap() for name, a in arrays.items()}
    out = nc.dram_tensor("out", (GROUPS, P, PER * D), F32, kind="ExternalOutput").ap()
    graph_layer(nc, aps["x"], aps["adj"], aps["w_t"], aps["bias"], out)
    r = run_bass_kernel_spmd(nc, [{name + "_in": a for name, a in arrays.items()}], core_ids=[0])
    return r.results[0]["out"].reshape(GROUPS, P, PER, D).transpose(0, 2, 1, 3).reshape(N, D)
```

```python
from contextlib import ExitStack

import concourse.bass as bass
from concourse import mybir

F32 = mybir.dt.float32
F32R = mybir.dt.float32r
ALU = mybir.AluOpType
ACT = mybir.ActivationFunctionType

P = 128
N = 8192
D = 128
EPS = 1e-5
BANK = 512
TILES = N // P
CHUNK = 2048
PER = CHUNK // BANK
GROUPS = TILES // PER
WIDE = CHUNK // BANK
STRIP_CHUNKS = TILES // PER
CHUNKS = TILES + (GROUPS - WIDE) * STRIP_CHUNKS
UNROLL = 3
BODY = UNROLL * STRIP_CHUNKS
LOOP_START = WIDE + 2
LAST = GROUPS - 1
ROUNDS = (LAST - LOOP_START) // UNROLL
RAW = 6
HI = 3
LO = 2
STAGES = 2
SLOTS = 3
HALF = BANK // 2
assert BODY % RAW == BODY % HI == BODY % LO == UNROLL % SLOTS == 0 and LOOP_START + ROUNDS * UNROLL == LAST

STATS = [(0, 4, None, 4), (4, 8, 0, 4), (8, 16, 1, 4), (16, 32, 3, 2), (32, 48, 11, 1), (48, 64, 27, 1)]


def gathered(i):
    a, b, first, rate = STATS[i]
    return first + (b - a) // rate - 1


def rooted(i):
    return gathered(i) + (1 if i == 1 else 2)


def inverted(i):
    return gathered(i) + (1 if i == 1 else 3)


assert all(inverted(i) < STATS[i][0] - 2 or i == 1 for i in range(1, len(STATS)))


def first_chunk(strip):
    return TILES + (strip - WIDE) * STRIP_CHUNKS


def bank_of(strip):
    return strip if strip < WIDE else WIDE + (strip - WIDE) % SLOTS


def graph_layer(nc, x, adj, w_t, bias, out):
    with ExitStack() as ctx:
        def sb(name, shape, dt=F32):
            return ctx.enter_context(nc.sbuf_tensor(name, shape, dt))

        def sem(name):
            return ctx.enter_context(nc.semaphore(name))

        base = sb("base", [P, TILES, D])
        h_hi = sb("h_hi", [P, TILES, D], F32R)
        h_lo = sb("h_lo", [P, TILES, D], F32R)
        raw = sb("raw", [P, RAW, CHUNK])
        a_hi = sb("a_hi", [P, HI, CHUNK], F32R)
        a_lo = sb("a_lo", [P, LO, CHUNK], F32R)
        h = sb("h", [P, STAGES, PER, D])
        h_t = sb("h_t", [P, PER * P])
        self_sb = sb("self_sb", [P, PER, D])
        strip_sb = sb("strip_sb", [P, SLOTS, BANK])
        w_self = sb("w_self", [P, D])
        w_neigh = sb("w_neigh", [P, D])
        bias_rows = sb("bias_rows", [P, D])
        identity = sb("identity", [P, P])
        moments = sb("moments", [P, TILES, 6])
        mean_var = sb("mean_var", [P, TILES, 2])
        var_eps = sb("var_eps", [P, TILES])
        std = sb("std", [P, TILES])
        guess = sb("guess", [P, TILES])
        scratch = sb("scratch", [P, TILES])
        rstd = sb("rstd", [P, TILES])
        shift = sb("shift", [P, TILES])

        psum = [ctx.enter_context(nc.psum_tensor(f"bank{i}", [P, BANK], F32)) for i in range(8)]
        half_ps = psum[0:2]
        turned_ps = psum[6]
        self_ps = psum[7]

        x_loaded = [sem(f"x_loaded{i}") for i in range(len(STATS))]
        consts_loaded = sem("consts_loaded")
        raw_loaded = [sem(f"raw_loaded{i}") for i in range(RAW)]
        out_stored = [sem(f"out_stored{i}") for i in range(SLOTS)]
        identity_zero = sem("identity_zero")
        identity_ready = sem("identity_ready")
        moments_ready = sem("moments_ready")
        mean_var_ready = sem("mean_var_ready")
        var_ready = sem("var_ready")
        std_ready = sem("std_ready")
        newton_step = sem("newton_step")
        norm_ready = sem("norm_ready")
        h_ready = sem("h_ready")
        h_hi_ready = sem("h_hi_ready")
        h_lo_ready = sem("h_lo_ready")
        turned = sem("turned")
        h_t_ready = sem("h_t_ready")
        self_done = sem("self_done")
        self_out = sem("self_out")
        base_step = sem("base_step")
        base_ready = sem("base_ready")
        hi_ready = sem("hi_ready")
        lo_ready = sem("lo_ready")
        chunk_used = sem("chunk_used")
        neigh_ready = sem("neigh_ready")
        projected = sem("projected")
        out_ready = sem("out_ready")
        piece_loaded = [sem(f"piece_loaded{i}") for i in range(PER)]
        half_neigh_ready = sem("half_neigh_ready")
        half_projected = sem("half_projected")
        half_out_ready = sem("half_out_ready")
        half_stored = sem("half_stored")

        block = ctx.enter_context(nc.Block())

        @block.sync
        def _(sp):
            def load_x(i):
                a, b, _, _ = STATS[i]
                sp.dma_start(base[:, a:b, :], x[:, a:b, :]).then_inc(x_loaded[i], 16)

            def load_chunk(c, slot, wait):
                if wait:
                    sp.wait_ge(lo_ready, c - RAW + 1)
                sp.dma_start(raw[:, slot, :], adj[c, :, :]).then_inc(raw_loaded[slot], 16)

            def strip_loads(strip, r, chunks):
                for k in range(chunks):
                    n = first_chunk(strip) + k
                    load_chunk(r * BODY + n, n % RAW, True)

            load_x(0)
            for c in range(TILES):
                load_chunk(c, c % RAW, c >= RAW)
                for i in range(1, len(STATS)):
                    if c == max(0, STATS[i][2] - 1):
                        load_x(i)
            for strip in range(WIDE, LOOP_START):
                strip_loads(strip, 0, STRIP_CHUNKS)
            with sp.Fori(0, ROUNDS) as r:
                for u in range(UNROLL):
                    strip_loads(LOOP_START + u, r, STRIP_CHUNKS)
            strip_loads(LAST, 0, STRIP_CHUNKS - 1)
            sp.wait_ge(lo_ready, CHUNKS - RAW)
            for n in range(PER):
                piece = slice(n * BANK, (n + 1) * BANK)
                sp.dma_start(raw[:, (CHUNKS - 1) % RAW, piece], adj[CHUNKS - 1, :, piece]).then_inc(piece_loaded[n], 16)
            for n in range(2):
                sp.wait_ge(half_out_ready, n + 1)
                half = slice(n * HALF, (n + 1) * HALF)
                sp.dma_start(out[LAST, :, half], strip_sb[:, LAST % SLOTS, half]).then_inc(half_stored, 16)
            for slot in range(SLOTS):
                sp.wait_ge(out_stored[slot], 16 * len(range(slot, LAST, SLOTS)))
            sp.wait_ge(half_stored, 2 * 16)

        @block.gpsimd
        def _(pool):
            nc.gpsimd.memset(identity[:], 0.0).then_inc(identity_zero, 1)
            pool.wait_ge(identity_zero, 1)
            nc.gpsimd.affine_select(out=identity[:], in_=identity[:], compare_op=ALU.not_equal, fill=1.0,
                                    base=0, pattern=[[-1, P]], channel_multiplier=1).then_inc(identity_ready, 1)
            pool.wait_ge(consts_loaded, 16 * 3)
            for g in range(GROUPS):
                rows = base[:, g * PER:(g + 1) * PER, :]
                pool.wait_ge(self_out, g + 1)
                nc.gpsimd.tensor_tensor(rows, rows, self_sb[:], ALU.add).then_inc(base_step, 1)
                pool.wait_ge(base_step, g + 1)
                for t in range(PER):
                    row = base[:, g * PER + t, :]
                    last = nc.gpsimd.tensor_tensor(row, row, bias_rows[:], ALU.add)
                last.then_inc(base_ready, 1)

            def store(strip, slot):
                pool.wait_ge(out_ready, strip + 1)
                pool.dma_start(out[strip, :, :], strip_sb[:, slot, :]).then_inc(out_stored[slot], 16)

            for strip in range(LOOP_START):
                store(strip, strip % SLOTS)
            with pool.Fori(0, ROUNDS) as r:
                for u in range(UNROLL):
                    store(r * UNROLL + (LOOP_START + u), (LOOP_START + u) % SLOTS)

        @block.scalar
        def _(act):
            act.dma_start(w_self[:], w_t[0:D, :]).then_inc(consts_loaded, 16)
            act.dma_start(w_neigh[:], w_t[D:2 * D, :]).then_inc(consts_loaded, 16)
            act.dma_start(bias_rows[:], bias.to_broadcast([P, D])).then_inc(consts_loaded, 16)

            def split_hi(c, raw_slot, loads, hi_slot, wait):
                act.wait_ge(raw_loaded[raw_slot], loads)
                if wait:
                    act.wait_ge(chunk_used, c - HI + 1)
                nc.scalar.copy(a_hi[:, hi_slot, :], raw[:, raw_slot, :]).then_inc(hi_ready, 1)

            def root(i):
                a, b, _, _ = STATS[i]
                act.wait_ge(var_ready, i + 1)
                nc.scalar.activation(std[:, a:b], var_eps[:, a:b], ACT.Sqrt).then_inc(std_ready, 1)

            def normalise(g):
                i = [n for n, (a, b, _, _) in enumerate(STATS) if a <= g * PER < b][0]
                act.wait_ge(norm_ready, i + 1)
                if g >= STAGES:
                    act.wait_ge(turned, g - STAGES + 1)
                    act.wait_ge(h_lo_ready, g - STAGES + 1)
                for n in range(PER):
                    t = g * PER + n
                    last = nc.scalar.activation(h[:, g % STAGES, n, :], base[:, t, :], ACT.Relu,
                                                bias=shift[:, t:t + 1], scale=rstd[:, t:t + 1])
                last.then_inc(h_ready, 1)
                act.wait_ge(h_ready, g + 1)
                nc.scalar.copy(h_hi[:, g * PER:(g + 1) * PER, :], h[:, g % STAGES, :, :]).then_inc(h_hi_ready, 1)

            def bring_self(g):
                act.wait_ge(self_done, g + 1)
                if g:
                    act.wait_ge(base_step, g)
                nc.scalar.copy(self_sb[:], self_ps[:].rearrange("p (t d) -> p t d", t=PER)).then_inc(self_out, 1)

            def bring_h_t(g):
                act.wait_ge(turned, g + 1)
                if g:
                    act.wait_ge(self_done, g)
                nc.scalar.copy(h_t[:], turned_ps[:]).then_inc(h_t_ready, 1)

            def bring_neigh(slot, bank, chunks, stores):
                act.wait_ge(chunk_used, chunks)
                if stores is not None:
                    act.wait_ge(out_stored[slot], stores)
                nc.scalar.copy(strip_sb[:, slot, :], psum[bank][:]).then_inc(neigh_ready, 1)

            root(0)
            normalise(0)
            for c in range(TILES):
                split_hi(c, c % RAW, 16 * (c // RAW + 1), c % HI, c >= HI)
                g, step = divmod(c, PER)
                for i in range(1, len(STATS)):
                    if c == rooted(i):
                        root(i)
                if step == 2 and g + 1 < GROUPS:
                    normalise(g + 1)
                if step == 3:
                    if g:
                        bring_self(g - 1)
                    bring_h_t(g)

            def strip_splits(strip, r, chunks):
                for k in range(chunks):
                    n = first_chunk(strip) + k
                    split_hi(r * BODY + n, n % RAW, r * (16 * BODY // RAW) + 16 * (n // RAW + 1), n % HI, True)
                    if strip == WIDE:
                        if k == 4:
                            bring_self(GROUPS - 1)
                        if 4 <= k < 3 + WIDE:
                            bring_neigh((k - 4) % SLOTS, bank_of(k - 4), TILES, None)
                        if k == 11:
                            bring_neigh((strip - 1) % SLOTS, bank_of(strip - 1), TILES, 16)
                    elif k == 4:
                        bring_neigh((strip - 1) % SLOTS, bank_of(strip - 1), r * BODY + first_chunk(strip),
                                    r * 16 + 16 * ((strip - 1) // SLOTS))

            for strip in range(WIDE, LOOP_START):
                strip_splits(strip, 0, STRIP_CHUNKS)
            with act.Fori(0, ROUNDS) as r:
                for u in range(UNROLL):
                    strip_splits(LOOP_START + u, r, STRIP_CHUNKS)
            strip_splits(LAST, 0, STRIP_CHUNKS - 1)
            act.wait_ge(chunk_used, CHUNKS - HI)
            for n in range(PER):
                piece = slice(n * BANK, (n + 1) * BANK)
                act.wait_ge(piece_loaded[n], 16)
                nc.scalar.copy(a_hi[:, (CHUNKS - 1) % HI, piece], raw[:, (CHUNKS - 1) % RAW, piece]).then_inc(hi_ready, 1)
            act.wait_ge(out_stored[LAST % SLOTS], 16 * (LAST // SLOTS))
            act.wait_ge(chunk_used, CHUNKS)
            for n in range(2):
                half = slice(n * HALF, (n + 1) * HALF)
                nc.scalar.copy(strip_sb[:, LAST % SLOTS, half], psum[bank_of(LAST)][:, half]).then_inc(half_neigh_ready, 1)

        @block.vector
        def _(dve):
            def split_lo(c, raw_slot, hi_slot, lo_slot, wait):
                dve.wait_ge(hi_ready, c + 1)
                if wait:
                    dve.wait_ge(chunk_used, c - LO + 1)
                nc.vector.tensor_tensor(a_lo[:, lo_slot, :], raw[:, raw_slot, :],
                                        a_hi[:, hi_slot, :].bitcast(F32), ALU.subtract).then_inc(lo_ready, 1)

            def gather(a, b):
                for t in range(a, b):
                    last = nc.vector.bn_stats(moments[:, t, :], base[:, t, :])
                last.then_inc(moments_ready, b - a)
                dve.wait_ge(moments_ready, b)
                for t in range(a, b):
                    last = nc.vector.bn_aggr(mean_var[:, t, :], moments[:, t, :])
                last.then_inc(mean_var_ready, b - a)

            def add_eps(i):
                a, b, _, _ = STATS[i]
                dve.wait_ge(mean_var_ready, b)
                nc.vector.tensor_scalar(var_eps[:, a:b], mean_var[:, a:b, 1], EPS, None, ALU.add).then_inc(var_ready, 1)

            def invert(i):
                a, b, _, _ = STATS[i]
                v, y, s = var_eps[:, a:b], guess[:, a:b], scratch[:, a:b]
                dve.wait_ge(std_ready, i + 1)
                nc.vector.reciprocal(y, std[:, a:b]).then_inc(newton_step, 1)
                dve.wait_ge(newton_step, 5 * i + 1)
                nc.vector.tensor_tensor(s, v, y, ALU.mult).then_inc(newton_step, 1)
                dve.wait_ge(newton_step, 5 * i + 2)
                nc.vector.tensor_tensor(s, s, y, ALU.mult).then_inc(newton_step, 1)
                dve.wait_ge(newton_step, 5 * i + 3)
                nc.vector.tensor_scalar(s, s, -0.5, 1.5, ALU.mult, ALU.add).then_inc(newton_step, 1)
                dve.wait_ge(newton_step, 5 * i + 4)
                nc.vector.tensor_tensor(rstd[:, a:b], y, s, ALU.mult).then_inc(newton_step, 1)
                dve.wait_ge(newton_step, 5 * i + 5)
                nc.vector.scalar_tensor_tensor(out=shift[:, a:b], in0=mean_var[:, a:b, 0], scalar=-1.0,
                                               in1=rstd[:, a:b], op0=ALU.mult, op1=ALU.mult).then_inc(norm_ready, 1)

            def normalised_lo(g):
                dve.wait_ge(h_hi_ready, g + 1)
                tiles = slice(g * PER, (g + 1) * PER)
                nc.vector.tensor_tensor(h_lo[:, tiles, :], h[:, g % STAGES, :, :], h_hi[:, tiles, :].bitcast(F32),
                                        ALU.subtract).then_inc(h_lo_ready, 1)

            def add_up(strip, slot, bank):
                dve.wait_ge(projected, strip + 1)
                tiles = base[:, bass.ds(strip * PER, PER), :]
                nc.vector.tensor_tensor(strip_sb[:, slot, :].rearrange("p (t d) -> p t d", t=PER),
                                        psum[bank][:].rearrange("p (t d) -> p t d", t=PER),
                                        tiles, ALU.add).then_inc(out_ready, 1)

            dve.wait_ge(x_loaded[0], 16)
            gather(*STATS[0][:2])
            add_eps(0)
            invert(0)
            normalised_lo(0)
            for c in range(TILES):
                split_lo(c, c % RAW, c % HI, c % LO, c >= LO)
                g, step = divmod(c, PER)
                for i in range(1, len(STATS)):
                    a, b, first, rate = STATS[i]
                    if first <= c <= gathered(i):
                        if c == first:
                            dve.wait_ge(x_loaded[i], 16)
                        gather(a + (c - first) * rate, a + (c - first + 1) * rate)
                    if c == gathered(i):
                        add_eps(i)
                    if c == inverted(i):
                        invert(i)
                if step == 2 and g + 1 < GROUPS:
                    normalised_lo(g + 1)

            def strip_splits(strip, r, chunks):
                for k in range(chunks):
                    n = first_chunk(strip) + k
                    split_lo(r * BODY + n, n % RAW, n % HI, n % LO, True)
                    if strip == WIDE:
                        if k == 7:
                            dve.wait_ge(base_ready, GROUPS)
                        if 7 <= k < 6 + WIDE:
                            add_up(k - 7, (k - 7) % SLOTS, bank_of(k - 7))
                        if k == 14:
                            add_up(strip - 1, (strip - 1) % SLOTS, bank_of(strip - 1))
                    elif k == 7:
                        add_up(r * UNROLL + (strip - 1), (strip - 1) % SLOTS, bank_of(strip - 1))

            for strip in range(WIDE, LOOP_START):
                strip_splits(strip, 0, STRIP_CHUNKS)
            with dve.Fori(0, ROUNDS) as r:
                for u in range(UNROLL):
                    strip_splits(LOOP_START + u, r, STRIP_CHUNKS)
            strip_splits(LAST, 0, STRIP_CHUNKS - 1)
            dve.wait_ge(chunk_used, CHUNKS - LO)
            for n in range(PER):
                piece = slice(n * BANK, (n + 1) * BANK)
                dve.wait_ge(hi_ready, CHUNKS + n)
                nc.vector.tensor_tensor(a_lo[:, (CHUNKS - 1) % LO, piece], raw[:, (CHUNKS - 1) % RAW, piece],
                                        a_hi[:, (CHUNKS - 1) % HI, piece].bitcast(F32), ALU.subtract).then_inc(lo_ready, 1)
            for n in range(2):
                half = slice(n * HALF, (n + 1) * HALF)
                dve.wait_ge(half_projected, n + 1)
                nc.vector.tensor_tensor(strip_sb[:, LAST % SLOTS, half], half_ps[n][:, half],
                                        base[:, LAST * PER + n * PER // 2:LAST * PER + (n + 1) * PER // 2, :]
                                        .rearrange("p t d -> p (t d)"), ALU.add).then_inc(half_out_ready, 1)

        @block.tensor
        def _(pe):
            def products(c, hi_slot, lo_slot, terms):
                pe.wait_ge(hi_ready, c + 1)
                for n, (tile, bank, first, _) in enumerate(terms):
                    nc.tensor.matmul(bank[:], h_hi[:, tile, :], a_hi[:, hi_slot, n * BANK:(n + 1) * BANK],
                                     start=first, stop=False)
                for n, (tile, bank, _, _) in enumerate(terms):
                    nc.tensor.matmul(bank[:], h_lo[:, tile, :], a_hi[:, hi_slot, n * BANK:(n + 1) * BANK],
                                     start=False, stop=False)
                pe.wait_ge(lo_ready, c + 1)
                for n, (tile, bank, _, last) in enumerate(terms):
                    mm = nc.tensor.matmul(bank[:], h_hi[:, tile, :], a_lo[:, lo_slot, n * BANK:(n + 1) * BANK],
                                          start=False, stop=last)
                mm.then_inc(chunk_used, 1)

            def turn(g):
                pe.wait_ge(h_ready, g + 1)
                if g:
                    pe.wait_ge(h_t_ready, g)
                for t in range(PER):
                    last = nc.tensor.transpose(turned_ps[:, t * P:(t + 1) * P], h[:, g % STAGES, t, :], identity[:])
                last.then_inc(turned, 1)

            def self_term(g):
                pe.wait_ge(h_t_ready, g + 1)
                if g:
                    pe.wait_ge(self_out, g)
                for t in range(PER):
                    last = nc.tensor.matmul(self_ps[:, t * D:(t + 1) * D], h_t[:, t * P:(t + 1) * P], w_self[:],
                                            start=True, stop=True)
                last.then_inc(self_done, 1)

            def project(strip, slot, bank):
                pe.wait_ge(neigh_ready, strip + 1)
                for t in range(PER):
                    last = nc.tensor.matmul(psum[bank][:, t * D:(t + 1) * D],
                                            strip_sb[:, slot, t * P:(t + 1) * P], w_neigh[:], start=True, stop=True)
                last.then_inc(projected, 1)

            pe.wait_ge(identity_ready, 1)
            turn(0)
            pe.wait_ge(consts_loaded, 16 * 3)
            pe.wait_ge(h_hi_ready, 1)
            pe.wait_ge(h_lo_ready, 1)
            for c in range(TILES):
                g, step = divmod(c, PER)
                if step == 0:
                    pe.wait_ge(h_hi_ready, g + 1)
                    pe.wait_ge(h_lo_ready, g + 1)
                products(c, c % HI, c % LO, [(c, psum[bank_of(s)], c == 0, c == TILES - 1) for s in range(WIDE)])
                if step == 3:
                    self_term(g)
                    if g + 1 < GROUPS:
                        turn(g + 1)

            def strip_products(strip, r, chunks, bank_wait):
                if bank_wait:
                    pe.wait_ge(out_ready, r * UNROLL + (strip - SLOTS + 1))
                for k in range(chunks):
                    n = first_chunk(strip) + k
                    products(r * BODY + n, n % HI, n % LO, [(t, psum[bank_of(strip)], t == 0, t == TILES - 1)
                                                            for t in range(k * PER, (k + 1) * PER)])
                    if strip == WIDE:
                        if 4 <= k < 3 + WIDE:
                            project(k - 4, (k - 4) % SLOTS, bank_of(k - 4))
                        if k == 11:
                            project(strip - 1, (strip - 1) % SLOTS, bank_of(strip - 1))
                    elif k == 4:
                        project(r * UNROLL + (strip - 1), (strip - 1) % SLOTS, bank_of(strip - 1))

            for strip in range(WIDE, LOOP_START):
                strip_products(strip, 0, STRIP_CHUNKS, False)
            with pe.Fori(0, ROUNDS) as r:
                for u in range(UNROLL):
                    strip_products(LOOP_START + u, r, STRIP_CHUNKS, LOOP_START + u >= WIDE + SLOTS)
            strip_products(LAST, 0, STRIP_CHUNKS - 1, True)
            bank = psum[bank_of(LAST)]
            for n in range(PER):
                tile, piece = TILES - PER + n, slice(n * BANK, (n + 1) * BANK)
                pe.wait_ge(hi_ready, CHUNKS + n)
                nc.tensor.matmul(bank[:], h_hi[:, tile, :], a_hi[:, (CHUNKS - 1) % HI, piece], start=False, stop=False)
                nc.tensor.matmul(bank[:], h_lo[:, tile, :], a_hi[:, (CHUNKS - 1) % HI, piece], start=False, stop=False)
                pe.wait_ge(lo_ready, CHUNKS + n)
                mm = nc.tensor.matmul(bank[:], h_hi[:, tile, :], a_lo[:, (CHUNKS - 1) % LO, piece],
                                      start=False, stop=(n == PER - 1))
            mm.then_inc(chunk_used, 1)
            for n in range(2):
                pe.wait_ge(half_neigh_ready, n + 1)
                for t in range(n * PER // 2, (n + 1) * PER // 2):
                    mm = nc.tensor.matmul(half_ps[n][:, t * D:(t + 1) * D], strip_sb[:, LAST % SLOTS, t * P:(t + 1) * P],
                                          w_neigh[:], start=True, stop=True)
                mm.then_inc(half_projected, 1)


def kernel(x, adj, L0_gnn_W, L0_gnn_b):
    import numpy as np
    import concourse.bacc as bacc
    from concourse.bass_utils import run_bass_kernel_spmd

    x, adj, w, b = np.asarray(x), np.asarray(adj), np.asarray(L0_gnn_W), np.asarray(L0_gnn_b)
    wide = N // GROUPS * WIDE
    arrays = {
        "x": np.ascontiguousarray(x.reshape(TILES, P, D).transpose(1, 0, 2)),
        "adj": np.concatenate([
            adj[:wide].T.reshape(TILES, P, CHUNK),
            adj[wide:].reshape(GROUPS - WIDE, BANK, STRIP_CHUNKS, PER, P).transpose(0, 2, 4, 3, 1)
            .reshape(CHUNKS - TILES, P, CHUNK),
        ]),
        "w_t": np.ascontiguousarray(w.T),
        "bias": b.reshape(1, D),
    }
    nc = bacc.Bacc("TRN2", target_bir_lowering=False, num_devices=1)
    aps = {name: nc.dram_tensor(name + "_in", a.shape, F32, kind="ExternalInput").ap() for name, a in arrays.items()}
    out = nc.dram_tensor("out", (GROUPS, P, PER * D), F32, kind="ExternalOutput").ap()
    graph_layer(nc, aps["x"], aps["adj"], aps["w_t"], aps["bias"], out)
    r = run_bass_kernel_spmd(nc, [{name + "_in": a for name, a in arrays.items()}], core_ids=[0])
    return r.results[0]["out"].reshape(GROUPS, P, PER, D).transpose(0, 2, 1, 3).reshape(N, D)
```

```python
from contextlib import ExitStack

import concourse.bass as bass
from concourse import mybir

F32 = mybir.dt.float32
F32R = mybir.dt.float32r
ALU = mybir.AluOpType
ACT = mybir.ActivationFunctionType

P = 128
N = 8192
D = 128
EPS = 1e-5
BANK = 512
TILES = N // P
CHUNK = 2048
PER = CHUNK // BANK
GROUPS = TILES // PER
WIDE = CHUNK // BANK
STRIP_CHUNKS = TILES // PER
CHUNKS = TILES + (GROUPS - WIDE) * STRIP_CHUNKS
UNROLL = 3
BODY = UNROLL * STRIP_CHUNKS
LOOP_START = WIDE + 2
LAST = GROUPS - 1
PIECED = 4
PIECES = [(c, n, slice(n * BANK, (n + 1) * BANK)) for c in range(CHUNKS - PIECED, CHUNKS) for n in range(PER)]
ROUNDS = (LAST - LOOP_START) // UNROLL
RAW = 6
HI = 3
LO = 2
STAGES = 2
SLOTS = 3
HALF = BANK // 2
assert BODY % RAW == BODY % HI == BODY % LO == UNROLL % SLOTS == 0 and LOOP_START + ROUNDS * UNROLL == LAST
assert PIECED <= RAW and PIECED <= STRIP_CHUNKS - 10

STATS = [(0, 4, None, 4), (4, 8, 0, 4), (8, 16, 1, 4), (16, 32, 3, 2), (32, 48, 11, 1), (48, 64, 27, 1)]


def gathered(i):
    a, b, first, rate = STATS[i]
    return first + (b - a) // rate - 1


def rooted(i):
    return gathered(i) + (1 if i == 1 else 2)


def inverted(i):
    return gathered(i) + (1 if i == 1 else 3)


assert all(inverted(i) < STATS[i][0] - 2 or i == 1 for i in range(1, len(STATS)))


def first_chunk(strip):
    return TILES + (strip - WIDE) * STRIP_CHUNKS


def bank_of(strip):
    return strip if strip < WIDE else WIDE + (strip - WIDE) % SLOTS


def graph_layer(nc, x, adj, w_t, bias, out):
    with ExitStack() as ctx:
        def sb(name, shape, dt=F32):
            return ctx.enter_context(nc.sbuf_tensor(name, shape, dt))

        def sem(name):
            return ctx.enter_context(nc.semaphore(name))

        base = sb("base", [P, TILES, D])
        h_hi = sb("h_hi", [P, TILES, D], F32R)
        h_lo = sb("h_lo", [P, TILES, D], F32R)
        raw = sb("raw", [P, RAW, CHUNK])
        a_hi = sb("a_hi", [P, HI, CHUNK], F32R)
        a_lo = sb("a_lo", [P, LO, CHUNK], F32R)
        h = sb("h", [P, STAGES, PER, D])
        h_t = sb("h_t", [P, PER * P])
        strip_sb = sb("strip_sb", [P, SLOTS, BANK])
        w_self = sb("w_self", [P, D])
        w_neigh = sb("w_neigh", [P, D])
        bias_rows = sb("bias_rows", [P, D])
        identity = sb("identity", [P, P])
        moments = sb("moments", [P, TILES, 6])
        mean_var = sb("mean_var", [P, TILES, 2])
        var_eps = sb("var_eps", [P, TILES])
        std = sb("std", [P, TILES])
        guess = sb("guess", [P, TILES])
        scratch = sb("scratch", [P, TILES])
        rstd = sb("rstd", [P, TILES])
        shift = sb("shift", [P, TILES])

        psum = [ctx.enter_context(nc.psum_tensor(f"bank{i}", [P, BANK], F32)) for i in range(8)]
        half_ps = psum[0:2]
        turned_ps = psum[6]
        self_ps = psum[7]

        x_loaded = [sem(f"x_loaded{i}") for i in range(len(STATS))]
        consts_loaded = sem("consts_loaded")
        raw_loaded = [sem(f"raw_loaded{i}") for i in range(RAW)]
        out_stored = [sem(f"out_stored{i}") for i in range(SLOTS)]
        identity_zero = sem("identity_zero")
        identity_ready = sem("identity_ready")
        moments_ready = sem("moments_ready")
        mean_var_ready = sem("mean_var_ready")
        var_ready = sem("var_ready")
        std_ready = sem("std_ready")
        newton_step = sem("newton_step")
        norm_ready = sem("norm_ready")
        h_ready = sem("h_ready")
        h_hi_ready = sem("h_hi_ready")
        h_lo_ready = sem("h_lo_ready")
        turned = sem("turned")
        h_t_ready = sem("h_t_ready")
        self_done = sem("self_done")
        self_added = sem("self_added")
        bias_added = sem("bias_added")
        hi_ready = sem("hi_ready")
        lo_ready = sem("lo_ready")
        chunk_used = sem("chunk_used")
        neigh_ready = sem("neigh_ready")
        projected = sem("projected")
        out_ready = sem("out_ready")
        piece_loaded = [sem(f"piece_loaded{i}") for i in range(len(PIECES))]
        half_neigh_ready = sem("half_neigh_ready")
        half_projected = sem("half_projected")
        half_out_ready = sem("half_out_ready")
        half_stored = sem("half_stored")

        block = ctx.enter_context(nc.Block())

        @block.sync
        def _(sp):
            def load_x(i):
                a, b, _, _ = STATS[i]
                sp.dma_start(base[:, a:b, :], x[:, a:b, :]).then_inc(x_loaded[i], 16)

            def load_chunk(c, slot, wait):
                if wait:
                    sp.wait_ge(lo_ready, c - RAW + 1)
                sp.dma_start(raw[:, slot, :], adj[c, :, :]).then_inc(raw_loaded[slot], 16)

            def strip_loads(strip, r, chunks):
                for k in range(chunks):
                    n = first_chunk(strip) + k
                    load_chunk(r * BODY + n, n % RAW, True)

            load_x(0)
            for c in range(TILES):
                load_chunk(c, c % RAW, c >= RAW)
                for i in range(1, len(STATS)):
                    if c == max(0, STATS[i][2] - 1):
                        load_x(i)
            for strip in range(WIDE, LOOP_START):
                strip_loads(strip, 0, STRIP_CHUNKS)
            with sp.Fori(0, ROUNDS) as r:
                for u in range(UNROLL):
                    strip_loads(LOOP_START + u, r, STRIP_CHUNKS)
            strip_loads(LAST, 0, STRIP_CHUNKS - PIECED)
            for m, (c, _, piece) in enumerate(PIECES):
                sp.wait_ge(lo_ready, c - RAW + 1)
                sp.dma_start(raw[:, c % RAW, piece], adj[c, :, piece]).then_inc(piece_loaded[m], 16)
            for n in range(2):
                sp.wait_ge(half_out_ready, n + 1)
                half = slice(n * HALF, (n + 1) * HALF)
                sp.dma_start(out[LAST, :, half], strip_sb[:, LAST % SLOTS, half]).then_inc(half_stored, 16)
            for slot in range(SLOTS):
                sp.wait_ge(out_stored[slot], 16 * len(range(slot, LAST, SLOTS)))
            sp.wait_ge(half_stored, 2 * 16)

        @block.gpsimd
        def _(pool):
            nc.gpsimd.memset(identity[:], 0.0).then_inc(identity_zero, 1)
            pool.wait_ge(identity_zero, 1)
            nc.gpsimd.affine_select(out=identity[:], in_=identity[:], compare_op=ALU.not_equal, fill=1.0,
                                    base=0, pattern=[[-1, P]], channel_multiplier=1).then_inc(identity_ready, 1)

            def store(strip, slot):
                pool.wait_ge(out_ready, strip + 1)
                pool.dma_start(out[strip, :, :], strip_sb[:, slot, :]).then_inc(out_stored[slot], 16)

            for strip in range(LOOP_START):
                store(strip, strip % SLOTS)
            with pool.Fori(0, ROUNDS) as r:
                for u in range(UNROLL):
                    store(r * UNROLL + (LOOP_START + u), (LOOP_START + u) % SLOTS)

        @block.scalar
        def _(act):
            act.dma_start(w_self[:], w_t[0:D, :]).then_inc(consts_loaded, 16)
            act.dma_start(w_neigh[:], w_t[D:2 * D, :]).then_inc(consts_loaded, 16)
            act.dma_start(bias_rows[:], bias.to_broadcast([P, D])).then_inc(consts_loaded, 16)

            def split_hi(c, raw_slot, loads, hi_slot, wait):
                act.wait_ge(raw_loaded[raw_slot], loads)
                if wait:
                    act.wait_ge(chunk_used, c - HI + 1)
                nc.scalar.copy(a_hi[:, hi_slot, :], raw[:, raw_slot, :]).then_inc(hi_ready, 1)

            def root(i):
                a, b, _, _ = STATS[i]
                act.wait_ge(var_ready, i + 1)
                nc.scalar.activation(std[:, a:b], var_eps[:, a:b], ACT.Sqrt).then_inc(std_ready, 1)

            def normalise(g):
                i = [n for n, (a, b, _, _) in enumerate(STATS) if a <= g * PER < b][0]
                act.wait_ge(norm_ready, i + 1)
                if g >= STAGES:
                    act.wait_ge(turned, g - STAGES + 1)
                    act.wait_ge(h_lo_ready, g - STAGES + 1)
                for n in range(PER):
                    t = g * PER + n
                    last = nc.scalar.activation(h[:, g % STAGES, n, :], base[:, t, :], ACT.Relu,
                                                bias=shift[:, t:t + 1], scale=rstd[:, t:t + 1])
                last.then_inc(h_ready, 1)
                act.wait_ge(h_ready, g + 1)
                nc.scalar.copy(h_hi[:, g * PER:(g + 1) * PER, :], h[:, g % STAGES, :, :]).then_inc(h_hi_ready, 1)

            def bring_h_t(g):
                act.wait_ge(turned, g + 1)
                if g:
                    act.wait_ge(self_done, g)
                nc.scalar.copy(h_t[:], turned_ps[:]).then_inc(h_t_ready, 1)

            def bring_neigh(slot, bank, chunks, stores):
                act.wait_ge(chunk_used, chunks)
                if stores is not None:
                    act.wait_ge(out_stored[slot], stores)
                nc.scalar.copy(strip_sb[:, slot, :], psum[bank][:]).then_inc(neigh_ready, 1)

            root(0)
            normalise(0)
            for c in range(TILES):
                split_hi(c, c % RAW, 16 * (c // RAW + 1), c % HI, c >= HI)
                g, step = divmod(c, PER)
                for i in range(1, len(STATS)):
                    if c == rooted(i):
                        root(i)
                if step == 2 and g + 1 < GROUPS:
                    normalise(g + 1)
                if step == 3:
                    bring_h_t(g)

            def strip_splits(strip, r, chunks):
                for k in range(chunks):
                    n = first_chunk(strip) + k
                    split_hi(r * BODY + n, n % RAW, r * (16 * BODY // RAW) + 16 * (n // RAW + 1), n % HI, True)
                    if strip == WIDE:
                        if 4 <= k < 3 + WIDE:
                            bring_neigh((k - 4) % SLOTS, bank_of(k - 4), TILES, None)
                        if k == 11:
                            bring_neigh((strip - 1) % SLOTS, bank_of(strip - 1), TILES, 16)
                    elif k == 4:
                        bring_neigh((strip - 1) % SLOTS, bank_of(strip - 1), r * BODY + first_chunk(strip),
                                    r * 16 + 16 * ((strip - 1) // SLOTS))

            for strip in range(WIDE, LOOP_START):
                strip_splits(strip, 0, STRIP_CHUNKS)
            with act.Fori(0, ROUNDS) as r:
                for u in range(UNROLL):
                    strip_splits(LOOP_START + u, r, STRIP_CHUNKS)
            strip_splits(LAST, 0, STRIP_CHUNKS - PIECED)
            for m, (c, _, piece) in enumerate(PIECES):
                act.wait_ge(chunk_used, c - HI + 1)
                act.wait_ge(piece_loaded[m], 16)
                nc.scalar.copy(a_hi[:, c % HI, piece], raw[:, c % RAW, piece]).then_inc(hi_ready, 1)
            act.wait_ge(out_stored[LAST % SLOTS], 16 * (LAST // SLOTS))
            act.wait_ge(chunk_used, CHUNKS)
            for n in range(2):
                half = slice(n * HALF, (n + 1) * HALF)
                nc.scalar.copy(strip_sb[:, LAST % SLOTS, half], psum[bank_of(LAST)][:, half]).then_inc(half_neigh_ready, 1)

        @block.vector
        def _(dve):
            def split_lo(c, raw_slot, hi_slot, lo_slot, wait):
                dve.wait_ge(hi_ready, c + 1)
                if wait:
                    dve.wait_ge(chunk_used, c - LO + 1)
                nc.vector.tensor_tensor(a_lo[:, lo_slot, :], raw[:, raw_slot, :],
                                        a_hi[:, hi_slot, :].bitcast(F32), ALU.subtract).then_inc(lo_ready, 1)

            def gather(a, b):
                for t in range(a, b):
                    last = nc.vector.bn_stats(moments[:, t, :], base[:, t, :])
                last.then_inc(moments_ready, b - a)
                dve.wait_ge(moments_ready, b)
                for t in range(a, b):
                    last = nc.vector.bn_aggr(mean_var[:, t, :], moments[:, t, :])
                last.then_inc(mean_var_ready, b - a)

            def add_eps(i):
                a, b, _, _ = STATS[i]
                dve.wait_ge(mean_var_ready, b)
                nc.vector.tensor_scalar(var_eps[:, a:b], mean_var[:, a:b, 1], EPS, None, ALU.add).then_inc(var_ready, 1)

            def invert(i):
                a, b, _, _ = STATS[i]
                v, y, s = var_eps[:, a:b], guess[:, a:b], scratch[:, a:b]
                dve.wait_ge(std_ready, i + 1)
                nc.vector.reciprocal(y, std[:, a:b]).then_inc(newton_step, 1)
                dve.wait_ge(newton_step, 5 * i + 1)
                nc.vector.tensor_tensor(s, v, y, ALU.mult).then_inc(newton_step, 1)
                dve.wait_ge(newton_step, 5 * i + 2)
                nc.vector.tensor_tensor(s, s, y, ALU.mult).then_inc(newton_step, 1)
                dve.wait_ge(newton_step, 5 * i + 3)
                nc.vector.tensor_scalar(s, s, -0.5, 1.5, ALU.mult, ALU.add).then_inc(newton_step, 1)
                dve.wait_ge(newton_step, 5 * i + 4)
                nc.vector.tensor_tensor(rstd[:, a:b], y, s, ALU.mult).then_inc(newton_step, 1)
                dve.wait_ge(newton_step, 5 * i + 5)
                nc.vector.scalar_tensor_tensor(out=shift[:, a:b], in0=mean_var[:, a:b, 0], scalar=-1.0,
                                               in1=rstd[:, a:b], op0=ALU.mult, op1=ALU.mult).then_inc(norm_ready, 1)

            def normalised_lo(g):
                dve.wait_ge(h_hi_ready, g + 1)
                tiles = slice(g * PER, (g + 1) * PER)
                nc.vector.tensor_tensor(h_lo[:, tiles, :], h[:, g % STAGES, :, :], h_hi[:, tiles, :].bitcast(F32),
                                        ALU.subtract).then_inc(h_lo_ready, 1)

            def add_self(g):
                dve.wait_ge(self_done, g + 1)
                rows = base[:, g * PER:(g + 1) * PER, :]
                nc.vector.tensor_tensor(rows, self_ps[:].rearrange("p (t d) -> p t d", t=PER), rows,
                                        ALU.add).then_inc(self_added, 1)

            def add_bias(strip):
                rows = base[:, bass.ds(strip * PER, PER), :]
                nc.vector.tensor_tensor(rows, rows, bias_rows[:].rearrange("p (t d) -> p t d", t=1)
                                        .to_broadcast([P, PER, D]), ALU.add).then_inc(bias_added, 1)

            def add_up(strip, slot, bank):
                dve.wait_ge(projected, strip + 1)
                dve.wait_ge(bias_added, strip + 1)
                tiles = base[:, bass.ds(strip * PER, PER), :]
                nc.vector.tensor_tensor(strip_sb[:, slot, :].rearrange("p (t d) -> p t d", t=PER),
                                        psum[bank][:].rearrange("p (t d) -> p t d", t=PER),
                                        tiles, ALU.add).then_inc(out_ready, 1)

            dve.wait_ge(x_loaded[0], 16)
            gather(*STATS[0][:2])
            add_eps(0)
            invert(0)
            normalised_lo(0)
            for c in range(TILES):
                split_lo(c, c % RAW, c % HI, c % LO, c >= LO)
                g, step = divmod(c, PER)
                for i in range(1, len(STATS)):
                    a, b, first, rate = STATS[i]
                    if first <= c <= gathered(i):
                        if c == first:
                            dve.wait_ge(x_loaded[i], 16)
                        gather(a + (c - first) * rate, a + (c - first + 1) * rate)
                    if c == gathered(i):
                        add_eps(i)
                    if c == inverted(i):
                        invert(i)
                if step == 2 and g + 1 < GROUPS:
                    normalised_lo(g + 1)
                if step == 2 and g:
                    add_self(g - 1)

            def strip_splits(strip, r, chunks):
                for k in range(chunks):
                    n = first_chunk(strip) + k
                    split_lo(r * BODY + n, n % RAW, n % HI, n % LO, True)
                    if strip == WIDE:
                        if k == 3:
                            add_self(GROUPS - 1)
                            dve.wait_ge(consts_loaded, 16 * 3)
                            dve.wait_ge(self_added, GROUPS)
                        if 3 <= k < 3 + WIDE:
                            add_bias(k - 3)
                        if 7 <= k < 6 + WIDE:
                            add_up(k - 7, (k - 7) % SLOTS, bank_of(k - 7))
                        if k == 14:
                            add_up(strip - 1, (strip - 1) % SLOTS, bank_of(strip - 1))
                    elif k == 5:
                        add_bias(r * UNROLL + (strip - 1))
                    elif k == 7:
                        add_up(r * UNROLL + (strip - 1), (strip - 1) % SLOTS, bank_of(strip - 1))
                    if strip == LAST and k == 9:
                        add_bias(strip)

            for strip in range(WIDE, LOOP_START):
                strip_splits(strip, 0, STRIP_CHUNKS)
            with dve.Fori(0, ROUNDS) as r:
                for u in range(UNROLL):
                    strip_splits(LOOP_START + u, r, STRIP_CHUNKS)
            strip_splits(LAST, 0, STRIP_CHUNKS - PIECED)
            for m, (c, _, piece) in enumerate(PIECES):
                dve.wait_ge(chunk_used, c - LO + 1)
                dve.wait_ge(hi_ready, CHUNKS - PIECED + m + 1)
                nc.vector.tensor_tensor(a_lo[:, c % LO, piece], raw[:, c % RAW, piece],
                                        a_hi[:, c % HI, piece].bitcast(F32), ALU.subtract).then_inc(lo_ready, 1)
            dve.wait_ge(bias_added, GROUPS)
            for n in range(2):
                half = slice(n * HALF, (n + 1) * HALF)
                dve.wait_ge(half_projected, n + 1)
                nc.vector.tensor_tensor(strip_sb[:, LAST % SLOTS, half], half_ps[n][:, half],
                                        base[:, LAST * PER + n * PER // 2:LAST * PER + (n + 1) * PER // 2, :]
                                        .rearrange("p t d -> p (t d)"), ALU.add).then_inc(half_out_ready, 1)

        @block.tensor
        def _(pe):
            def products(c, hi_slot, lo_slot, terms):
                pe.wait_ge(hi_ready, c + 1)
                for n, (tile, bank, first, _) in enumerate(terms):
                    nc.tensor.matmul(bank[:], h_hi[:, tile, :], a_hi[:, hi_slot, n * BANK:(n + 1) * BANK],
                                     start=first, stop=False)
                for n, (tile, bank, _, _) in enumerate(terms):
                    nc.tensor.matmul(bank[:], h_lo[:, tile, :], a_hi[:, hi_slot, n * BANK:(n + 1) * BANK],
                                     start=False, stop=False)
                pe.wait_ge(lo_ready, c + 1)
                for n, (tile, bank, _, last) in enumerate(terms):
                    mm = nc.tensor.matmul(bank[:], h_hi[:, tile, :], a_lo[:, lo_slot, n * BANK:(n + 1) * BANK],
                                          start=False, stop=last)
                mm.then_inc(chunk_used, 1)

            def turn(g):
                pe.wait_ge(h_ready, g + 1)
                if g:
                    pe.wait_ge(h_t_ready, g)
                for t in range(PER):
                    last = nc.tensor.transpose(turned_ps[:, t * P:(t + 1) * P], h[:, g % STAGES, t, :], identity[:])
                last.then_inc(turned, 1)

            def self_term(g):
                pe.wait_ge(h_t_ready, g + 1)
                if g:
                    pe.wait_ge(self_added, g)
                for t in range(PER):
                    last = nc.tensor.matmul(self_ps[:, t * D:(t + 1) * D], h_t[:, t * P:(t + 1) * P], w_self[:],
                                            start=True, stop=True)
                last.then_inc(self_done, 1)

            def project(strip, slot, bank):
                pe.wait_ge(neigh_ready, strip + 1)
                for t in range(PER):
                    last = nc.tensor.matmul(psum[bank][:, t * D:(t + 1) * D],
                                            strip_sb[:, slot, t * P:(t + 1) * P], w_neigh[:], start=True, stop=True)
                last.then_inc(projected, 1)

            pe.wait_ge(identity_ready, 1)
            turn(0)
            pe.wait_ge(consts_loaded, 16 * 3)
            pe.wait_ge(h_hi_ready, 1)
            pe.wait_ge(h_lo_ready, 1)
            for c in range(TILES):
                g, step = divmod(c, PER)
                if step == 0:
                    pe.wait_ge(h_hi_ready, g + 1)
                    pe.wait_ge(h_lo_ready, g + 1)
                products(c, c % HI, c % LO, [(c, psum[bank_of(s)], c == 0, c == TILES - 1) for s in range(WIDE)])
                if step == 3:
                    self_term(g)
                    if g + 1 < GROUPS:
                        turn(g + 1)

            def strip_products(strip, r, chunks, bank_wait):
                if bank_wait:
                    pe.wait_ge(out_ready, r * UNROLL + (strip - SLOTS + 1))
                for k in range(chunks):
                    n = first_chunk(strip) + k
                    products(r * BODY + n, n % HI, n % LO, [(t, psum[bank_of(strip)], t == 0, t == TILES - 1)
                                                            for t in range(k * PER, (k + 1) * PER)])
                    if strip == WIDE:
                        if 4 <= k < 3 + WIDE:
                            project(k - 4, (k - 4) % SLOTS, bank_of(k - 4))
                        if k == 11:
                            project(strip - 1, (strip - 1) % SLOTS, bank_of(strip - 1))
                    elif k == 4:
                        project(r * UNROLL + (strip - 1), (strip - 1) % SLOTS, bank_of(strip - 1))

            for strip in range(WIDE, LOOP_START):
                strip_products(strip, 0, STRIP_CHUNKS, False)
            with pe.Fori(0, ROUNDS) as r:
                for u in range(UNROLL):
                    strip_products(LOOP_START + u, r, STRIP_CHUNKS, LOOP_START + u >= WIDE + SLOTS)
            strip_products(LAST, 0, STRIP_CHUNKS - PIECED, True)
            bank = psum[bank_of(LAST)]
            for m, (c, n, piece) in enumerate(PIECES):
                tile = TILES - len(PIECES) + m
                pe.wait_ge(hi_ready, CHUNKS - PIECED + m + 1)
                nc.tensor.matmul(bank[:], h_hi[:, tile, :], a_hi[:, c % HI, piece], start=False, stop=False)
                nc.tensor.matmul(bank[:], h_lo[:, tile, :], a_hi[:, c % HI, piece], start=False, stop=False)
                pe.wait_ge(lo_ready, CHUNKS - PIECED + m + 1)
                mm = nc.tensor.matmul(bank[:], h_hi[:, tile, :], a_lo[:, c % LO, piece],
                                      start=False, stop=(tile == TILES - 1))
                if n == PER - 1:
                    mm.then_inc(chunk_used, 1)
            for n in range(2):
                pe.wait_ge(half_neigh_ready, n + 1)
                for t in range(n * PER // 2, (n + 1) * PER // 2):
                    mm = nc.tensor.matmul(half_ps[n][:, t * D:(t + 1) * D], strip_sb[:, LAST % SLOTS, t * P:(t + 1) * P],
                                          w_neigh[:], start=True, stop=True)
                mm.then_inc(half_projected, 1)


def kernel(x, adj, L0_gnn_W, L0_gnn_b):
    import numpy as np
    import concourse.bacc as bacc
    from concourse.bass_utils import run_bass_kernel_spmd

    x, adj, w, b = np.asarray(x), np.asarray(adj), np.asarray(L0_gnn_W), np.asarray(L0_gnn_b)
    wide = N // GROUPS * WIDE
    arrays = {
        "x": np.ascontiguousarray(x.reshape(TILES, P, D).transpose(1, 0, 2)),
        "adj": np.concatenate([
            adj[:wide].T.reshape(TILES, P, CHUNK),
            adj[wide:].reshape(GROUPS - WIDE, BANK, STRIP_CHUNKS, PER, P).transpose(0, 2, 4, 3, 1)
            .reshape(CHUNKS - TILES, P, CHUNK),
        ]),
        "w_t": np.ascontiguousarray(w.T),
        "bias": b.reshape(1, D),
    }
    nc = bacc.Bacc("TRN2", target_bir_lowering=False, num_devices=1)
    aps = {name: nc.dram_tensor(name + "_in", a.shape, F32, kind="ExternalInput").ap() for name, a in arrays.items()}
    out = nc.dram_tensor("out", (GROUPS, P, PER * D), F32, kind="ExternalOutput").ap()
    graph_layer(nc, aps["x"], aps["adj"], aps["w_t"], aps["bias"], out)
    r = run_bass_kernel_spmd(nc, [{name + "_in": a for name, a in arrays.items()}], core_ids=[0])
    return r.results[0]["out"].reshape(GROUPS, P, PER, D).transpose(0, 2, 1, 3).reshape(N, D)
```
